# Optimizing a Trainium2 kernel written in Bass

```python
import numpy as np
import jax
import jax.numpy as jnp

def _softmax(x, axis=-1):
    return jax.nn.softmax(x, axis=axis)

def _gelu(x):
    return jax.nn.gelu(x, approximate=True)

def _silu(x):
    return jax.nn.silu(x)

def _sigmoid(x):
    return jax.nn.sigmoid(x)

def _layernorm(x, axis=-1, eps=1e-05):
    m = jnp.mean(x, axis=axis, keepdims=True)
    v = jnp.var(x, axis=axis, keepdims=True)
    return (x - m) / jnp.sqrt(v + eps)

def _scatter_add(tgt, idx, src, axis=0):
    return tgt.at[idx].add(src)

def _segment_sum(src, seg, n):
    return jax.ops.segment_sum(src, seg, n)
kernel_name = 'mk_rec_standalone_d1_rec_r8_79db5d'

def setup_inputs(seed: int=0):
    np.random.seed(seed)
    _w = jnp.asarray

    def _rec_inputs():
        import jax
        import jax.numpy as jnp
        _rk = jax.random.key(seed)
        r_feats = -0.000596345 + 1.00056 * jax.random.normal(jax.random.fold_in(_rk, 1), (512, 128, 12), jnp.float32)
        return r_feats
    r_feats = _rec_inputs()

    def _L0_rec_setup():
        import jax, jax.numpy as jnp
        import numpy as np
        B, N, HID = (256, 128, 128)
        N_FLAT, N_PATH = (4, 8)
        DELTA_IDX = 3
        NEG = 0.2

        def _leaky(x):
            return jnp.where(x >= 0, x, NEG * x)

        def _tower(x, w_in, b_in, blocks):
            h = _leaky(x @ w_in + b_in)
            for w1, b1, w2, b2 in blocks:
                h = _leaky(_leaky(h @ w1 + b1) @ w2 + b2 + h)
            return h
        key = jax.random.key(seed)
        ks = iter(jax.random.split(key, 32))

        def W(i, o):
            return jax.random.normal(next(ks), (i, o), jnp.float32) / np.float32(np.sqrt(i))

        def bvec(o):
            return jax.random.normal(next(ks), (o,), jnp.float32) * 0.01
        inp = {'feats': jax.random.normal(next(ks), (B, N, N_FLAT + N_PATH), jnp.float32)}
        inp.update(fw_in=W(N_FLAT, HID), fb_in=bvec(HID), fr1_w1=W(HID, HID), fr1_b1=bvec(HID), fr1_w2=W(HID, HID), fr1_b2=bvec(HID), fr2_w1=W(HID, HID), fr2_b1=bvec(HID), fr2_w2=W(HID, HID), fr2_b2=bvec(HID))
        inp.update(pw_in=W(N_PATH, HID), pb_in=bvec(HID), pr1_w1=W(HID, HID), pr1_b1=bvec(HID), pr1_w2=W(HID, HID), pr1_b2=bvec(HID), pr2_w1=W(HID, HID), pr2_b1=bvec(HID), pr2_w2=W(HID, HID), pr2_b2=bvec(HID))
        inp.update(cw1=W(2 * HID, HID), cb1=bvec(HID), cw2=W(HID, 1), cb2=bvec(1))
        return inp
    _L0_rec_all = _L0_rec_setup()
    _L0_rec_in = {k: v for k, v in _L0_rec_all.items() if k in ('fw_in', 'fb_in', 'fr1_w1', 'fr1_b1', 'fr1_w2', 'fr1_b2', 'fr2_w1', 'fr2_b1', 'fr2_w2', 'fr2_b2', 'pw_in', 'pb_in', 'pr1_w1', 'pr1_b1', 'pr1_w2', 'pr1_b2', 'pr2_w1', 'pr2_b1', 'pr2_w2', 'pr2_b2', 'cw1', 'cb1', 'cw2', 'cb2')}
    del _L0_rec_all
    return {'r_feats': r_feats, 'L0_rec_fw_in': _L0_rec_in['fw_in'], 'L0_rec_fb_in': _L0_rec_in['fb_in'], 'L0_rec_fr1_w1': _L0_rec_in['fr1_w1'], 'L0_rec_fr1_b1': _L0_rec_in['fr1_b1'], 'L0_rec_fr1_w2': _L0_rec_in['fr1_w2'], 'L0_rec_fr1_b2': _L0_rec_in['fr1_b2'], 'L0_rec_fr2_w1': _L0_rec_in['fr2_w1'], 'L0_rec_fr2_b1': _L0_rec_in['fr2_b1'], 'L0_rec_fr2_w2': _L0_rec_in['fr2_w2'], 'L0_rec_fr2_b2': _L0_rec_in['fr2_b2'], 'L0_rec_pw_in': _L0_rec_in['pw_in'], 'L0_rec_pb_in': _L0_rec_in['pb_in'], 'L0_rec_pr1_w1': _L0_rec_in['pr1_w1'], 'L0_rec_pr1_b1': _L0_rec_in['pr1_b1'], 'L0_rec_pr1_w2': _L0_rec_in['pr1_w2'], 'L0_rec_pr1_b2': _L0_rec_in['pr1_b2'], 'L0_rec_pr2_w1': _L0_rec_in['pr2_w1'], 'L0_rec_pr2_b1': _L0_rec_in['pr2_b1'], 'L0_rec_pr2_w2': _L0_rec_in['pr2_w2'], 'L0_rec_pr2_b2': _L0_rec_in['pr2_b2'], 'L0_rec_cw1': _L0_rec_in['cw1'], 'L0_rec_cb1': _L0_rec_in['cb1'], 'L0_rec_cw2': _L0_rec_in['cw2'], 'L0_rec_cb2': _L0_rec_in['cb2']}

def reference(r_feats, L0_rec_fw_in, L0_rec_fb_in, L0_rec_fr1_w1, L0_rec_fr1_b1, L0_rec_fr1_w2, L0_rec_fr1_b2, L0_rec_fr2_w1, L0_rec_fr2_b1, L0_rec_fr2_w2, L0_rec_fr2_b2, L0_rec_pw_in, L0_rec_pb_in, L0_rec_pr1_w1, L0_rec_pr1_b1, L0_rec_pr1_w2, L0_rec_pr1_b2, L0_rec_pr2_w1, L0_rec_pr2_b1, L0_rec_pr2_w2, L0_rec_pr2_b2, L0_rec_cw1, L0_rec_cb1, L0_rec_cw2, L0_rec_cb2):
    import jax
    import jax.numpy as jnp

    def _L0_rec_ref(feats, fw_in, fb_in, fr1_w1, fr1_b1, fr1_w2, fr1_b2, fr2_w1, fr2_b1, fr2_w2, fr2_b2, pw_in, pb_in, pr1_w1, pr1_b1, pr1_w2, pr1_b2, pr2_w1, pr2_b1, pr2_w2, pr2_b2, cw1, cb1, cw2, cb2):
        import jax, jax.numpy as jnp
        import numpy as np
        B, N, HID = (256, 128, 128)
        N_FLAT, N_PATH = (4, 8)
        DELTA_IDX = 3
        NEG = 0.2

        def _leaky(x):
            return jnp.where(x >= 0, x, NEG * x)

        def _tower(x, w_in, b_in, blocks):
            h = _leaky(x @ w_in + b_in)
            for w1, b1, w2, b2 in blocks:
                h = _leaky(_leaky(h @ w1 + b1) @ w2 + b2 + h)
            return h
        batch, n, _ = feats.shape
        flat_blocks = [(fr1_w1, fr1_b1, fr1_w2, fr1_b2), (fr2_w1, fr2_b1, fr2_w2, fr2_b2)]
        path_blocks = [(pr1_w1, pr1_b1, pr1_w2, pr1_b2), (pr2_w1, pr2_b1, pr2_w2, pr2_b2)]

        def step(prev_delta, xk):
            fk, k = xk
            d = jnp.where(k == 0, fk[:, DELTA_IDX], jax.lax.stop_gradient(prev_delta))
            fk = fk.at[:, DELTA_IDX].set(d)
            fe = _tower(fk[:, :N_FLAT], fw_in, fb_in, flat_blocks)
            pe = _tower(fk[:, N_FLAT:], pw_in, pb_in, path_blocks)
            h = _leaky(jnp.concatenate([fe, pe], axis=-1) @ cw1 + cb1)
            delta = jax.nn.sigmoid(h @ cw2 + cb2)[:, 0]
            return (delta, delta)
        xs = (jnp.swapaxes(feats, 0, 1), jnp.arange(n))
        _, deltas = jax.lax.scan(step, jnp.zeros((batch,), feats.dtype), xs)
        return jnp.swapaxes(deltas, 0, 1)
    y = _L0_rec_ref(r_feats, L0_rec_fw_in, L0_rec_fb_in, L0_rec_fr1_w1, L0_rec_fr1_b1, L0_rec_fr1_w2, L0_rec_fr1_b2, L0_rec_fr2_w1, L0_rec_fr2_b1, L0_rec_fr2_w2, L0_rec_fr2_b2, L0_rec_pw_in, L0_rec_pb_in, L0_rec_pr1_w1, L0_rec_pr1_b1, L0_rec_pr1_w2, L0_rec_pr1_b2, L0_rec_pr2_w1, L0_rec_pr2_b1, L0_rec_pr2_w2, L0_rec_pr2_b2, L0_rec_cw1, L0_rec_cb1, L0_rec_cw2, L0_rec_cb2)
    return y

_drawn_inputs = setup_inputs


def setup_inputs(seed=0):
    import zlib

    import numpy as np

    out = dict(_drawn_inputs(seed))
    spreads = {}
    factors = {'L0_rec_fb_in': 23.907,
     'L0_rec_fr1_b1': 46.548,
     'L0_rec_fr1_b2': 32.406,
     'L0_rec_fr2_b1': 8.0,
     'L0_rec_fr2_b2': 8.0,
     'L0_rec_pb_in': 25.603,
     'L0_rec_pr1_b1': 32.746,
     'L0_rec_pr1_b2': 30.726,
     'L0_rec_pr2_b1': 35.856,
     'L0_rec_pr2_b2': 31.703,
     'L0_rec_cb1': 30.625}
    for name, (base, spread) in spreads.items():
        noise = np.random.default_rng([zlib.crc32(name.encode()), seed]).standard_normal(out[name].shape)
        drawn = base * np.exp(spread * noise) if base else spread * noise
        out[name] = jnp.asarray(drawn.astype(out[name].dtype))
    for name, factor in factors.items():
        out[name] = (out[name] * factor).astype(out[name].dtype)
    return out
```

```python
import numpy as np

import concourse.bass as bass
from concourse import mybir
from contextlib import ExitStack

STEPS, BATCH, FEATS, HID = 128, 512, 12, 128
N_FLAT, DELTA = 4, 3
NEG = 0.2
GROUPS = 2
G = BATCH // GROUPS
QUAD = 32
CHUNKS = 4
CHUNK_STEPS = STEPS // CHUNKS
CHUNK_COLS = CHUNK_STEPS * FEATS * BATCH // 128
AHEAD = 3

HIDDEN = ["fr1_w1", "fr1_w2", "fr2_w1", "fr2_w2", "pr1_w1", "pr1_w2", "pr2_w1", "pr2_w2"]
BIASES = ["fr1_b1", "fr1_b2", "fr2_b1", "fr2_b2", "pr1_b1", "pr1_b2", "pr2_b1", "pr2_b2", "cb1", "cb2"]


def build(nc, x, x_hi, x_lo, w, out):
    fp32, fp32r = mybir.dt.float32, mybir.dt.float32r
    ALU, ACT = mybir.AluOpType, mybir.ActivationFunctionType

    ctx = ExitStack()
    with ctx:
        def sb(name, shape, dt=fp32):
            return ctx.enter_context(nc.sbuf_tensor(name, shape, dt))

        def bank(name):
            return ctx.enter_context(nc.psum_tensor(name, [128, 512], fp32))

        def sem(name):
            return ctx.enter_context(nc.semaphore(name))

        def per_group(name):
            return [sem(f"{name}_{g}") for g in range(GROUPS)]

        hidden = {n: sb(n, [HID, HID]) for n in HIDDEN}
        comb_flat, comb_path = sb("comb_flat", [HID, HID]), sb("comb_path", [HID, HID])
        bias = {n: sb(n + "_col", [HID, 1]) for n in BIASES}
        cw2_col, cw2_rep = sb("cw2_col", [HID, 1]), sb("cw2_rep", [HID, HID])
        delta_w = sb("delta_w", [HID, 1])
        in_raw = {t: sb(f"in_raw_{t}", [128, HID]) for t in "fp"}
        in_split = {t: sb(f"in_split_{t}", [128, HID], fp32r) for t in "fp"}
        chunk_x = [sb(f"chunk_x{c}", [128, CHUNK_COLS]) for c in range(CHUNKS)]
        chunk_hi = [sb(f"chunk_hi{c}", [128, CHUNK_COLS], fp32r) for c in range(CHUNKS)]
        chunk_lo = [sb(f"chunk_lo{c}", [128, CHUNK_COLS], fp32r) for c in range(CHUNKS)]
        x_split = [sb(f"x_split{p}", [128, BATCH], fp32r) for p in range(2)]
        p_in, p_mid1, p_mid2 = sb("p_in", [HID, BATCH]), sb("p_mid1", [HID, BATCH]), sb("p_mid2", [HID, BATCH])
        p_t1, p_t2 = sb("p_t1", [HID, BATCH]), sb("p_t2", [HID, BATCH])
        p_sum1, p_sum2 = sb("p_sum1", [HID, BATCH]), sb("p_sum2", [HID, BATCH])
        p_res1 = [sb(f"p_res1_{p}", [HID, BATCH]) for p in range(2)]
        p_res2 = [sb(f"p_res2_{p}", [HID, BATCH]) for p in range(2)]
        f_t, f_in, f_mid1, f_mid2, f_res1, f_res2, head = (
            [sb(f"{n}_{g}", [HID, G]) for g in range(GROUPS)]
            for n in ("f_t", "f_in", "f_mid1", "f_mid2", "f_res1", "f_res2", "head"))
        delta = [sb(f"delta{p}", [HID, BATCH]) for p in range(2)]

        ps_flat = [bank(f"ps_flat{g}") for g in range(GROUPS)]
        ps_head = [bank(f"ps_head{g}") for g in range(GROUPS)]
        ps_path1, ps_path2 = bank("ps_path1"), bank("ps_path2")

        def layer(b, g):
            return b[g][:, 0:G]

        def second(b, g):
            return b[g][:, G:2 * G]

        def cols(t, g):
            return t[:, g * G:(g + 1) * G]

        s_pads, s_in_zero, s_in_loaded, s_w_loaded, s_b_loaded = (
            sem("s_pads"), sem("s_in_zero"), sem("s_in_loaded"), sem("s_w_loaded"), sem("s_b_loaded"))
        s_in_hi, s_in_split, s_cw2, s_delta0 = sem("s_in_hi"), sem("s_in_split"), sem("s_cw2"), sem("s_delta0")
        s_chunk_loaded, s_chunk_hi, s_chunk_split, s_chunk_stored = (
            [sem(f"{n}{c}") for c in range(CHUNKS)]
            for n in ("s_chunk_loaded", "s_chunk_hi", "s_chunk_split", "s_chunk_stored"))
        s_x_loaded = [sem(f"s_x_loaded{p}") for p in range(2)]
        s_stored = sem("s_stored")
        s_p_in_mm, s_p_in_t, s_p_in_h, s_p1a_mm, s_p1a_t, s_p1a_h, s_p1b_mm, s_p1b_t, s_p1b_h = (sem(n) for n in (
            "s_p_in_mm", "s_p_in_t", "s_p_in_h", "s_p1a_mm", "s_p1a_t", "s_p1a_h", "s_p1b_mm", "s_p1b_t", "s_p1b_h"))
        s_p2a_mm, s_p2a_t, s_p2a_h, s_p2b_mm, s_p2b_t, s_p2b_h = (sem(n) for n in (
            "s_p2a_mm", "s_p2a_t", "s_p2a_h", "s_p2b_mm", "s_p2b_t", "s_p2b_h"))
        s_f_in_mm, s_f_in_t, s_f_in_h, s_f1a_mm, s_f1a_t, s_f1a_h, s_f1b_mm, s_f1b_t, s_f1b_h = (
            per_group(n) for n in ("s_f_in_mm", "s_f_in_t", "s_f_in_h", "s_f1a_mm", "s_f1a_t", "s_f1a_h",
                                   "s_f1b_mm", "s_f1b_t", "s_f1b_h"))
        s_f2a_mm, s_f2a_t, s_f2a_h, s_f2b_mm, s_f2b_t, s_f2b_h = (
            per_group(n) for n in ("s_f2a_mm", "s_f2a_t", "s_f2a_h", "s_f2b_mm", "s_f2b_t", "s_f2b_h"))
        s_head_mm, s_head_t, s_head_h, s_out_mm, s_delta = (
            per_group(n) for n in ("s_head_mm", "s_head_t", "s_head_h", "s_out_mm", "s_delta"))

        N_W, N_B, N_IN = 16 * (len(HIDDEN) + 2), 16 * (len(BIASES) + 2), 16 * 16

        x_rows = x.rearrange("s f b -> (s f b)").rearrange("(r n) -> r n", n=CHUNK_COLS)
        hi_rows = x_hi.rearrange("s f b -> (s f b)").rearrange("(r n) -> r n", n=CHUNK_COLS)
        lo_rows = x_lo.rearrange("s f b -> (s f b)").rearrange("(r n) -> r n", n=CHUNK_COLS)

        block = ctx.enter_context(nc.Block())

        def over_steps(eng, step):
            step(0, 0, True, True)
            step(1, 1, True, True)
            with eng.Fori(2, STEPS - 3, 2) as k:
                step(k, 0, True, True)
                step(k + 1, 1, True, True)
            step(STEPS - 2, 0, False, True)
            step(STEPS - 1, 1, False, False)

        @block.sync
        def _(sp):
            def load_x(k, par):
                if not (isinstance(k, int) and k < 2):
                    sp.wait_ge(s_p_in_mm, k - 1)
                    for g in range(GROUPS):
                        sp.wait_ge(s_f_in_mm[g], k - 1)
                for q, part in enumerate((x_hi, x_hi, x_lo, x_lo)):
                    sp.dma_start(x_split[par][q * QUAD:q * QUAD + FEATS, :].bitcast(fp32),
                                 part[bass.ds(k, 1), :, :].rearrange("a f b -> (a f) b")).then_inc(s_x_loaded[par], 16)

            def store_delta(k, par):
                for g in range(GROUPS):
                    sp.wait_ge(s_delta[g], k + 1)
                sp.dma_start(out[bass.ds(k, 1), :], delta[par][0:1, :]).then_inc(s_stored, 16)

            def store_chunk(c):
                sp.wait_ge(s_chunk_split[c], 1)
                sp.dma_start(hi_rows[c * 128:(c + 1) * 128, :], chunk_hi[c][:, :].bitcast(fp32)).then_inc(s_chunk_stored[c], 16)
                sp.dma_start(lo_rows[c * 128:(c + 1) * 128, :], chunk_lo[c][:, :].bitcast(fp32)).then_inc(s_chunk_stored[c], 16)

            def load_chunk(c):
                sp.dma_start(chunk_x[c][:, :], x_rows[c * 128:(c + 1) * 128, :]).then_inc(s_chunk_loaded[c], 16)

            load_chunk(0)
            for n in HIDDEN:
                sp.dma_start(hidden[n][:, :], w[n]).then_inc(s_w_loaded, 16)
            sp.dma_start(comb_flat[:, :], w["cw1"][0:HID, :]).then_inc(s_w_loaded, 16)
            sp.dma_start(comb_path[:, :], w["cw1"][HID:2 * HID, :]).then_inc(s_w_loaded, 16)
            sp.dma_start(delta[1][:, :], x[0, DELTA:DELTA + 1, :].to_broadcast([HID, BATCH])).then_inc(s_delta0, 16)
            for c in range(1, CHUNKS):
                load_chunk(c)
            store_chunk(0)
            sp.wait_ge(s_pads, 2)
            for c in range(CHUNKS):
                sp.wait_ge(s_chunk_stored[c], 32)
                first = c * CHUNK_STEPS
                if c == 0:
                    for k in range(AHEAD):
                        load_x(k, k % 2)
                    store_first = AHEAD
                    for k in range(AHEAD, AHEAD + 1):
                        load_x(k, k % 2)
                        store_delta(k - AHEAD, (k - AHEAD) % 2)
                    first = AHEAD + 1
                    for later in range(1, CHUNKS):
                        store_chunk(later)
                with sp.Fori(first, (c + 1) * CHUNK_STEPS - 1, 2) as k:
                    for n in range(2):
                        load_x(k + n, n)
                        store_delta(k + n - AHEAD, 1 - n)
            for k in range(STEPS - AHEAD, STEPS):
                store_delta(k, k % 2)
            sp.wait_ge(s_stored, 16 * STEPS)

        @block.gpsimd
        def _(pool):
            for t in "fp":
                last = pool.memset(in_raw[t][:, :], 0.0)
            last.then_inc(s_in_zero, 1)
            for p in range(2):
                last = pool.memset(x_split[p][:, :].bitcast(fp32), 0.0)
            last.then_inc(s_pads, 1)
            pool.wait_ge(s_pads, 1)
            for p in range(2):
                last = pool.memset(x_split[p][0:2 * QUAD, :].bitcast(fp32), 1.0)
            last.then_inc(s_pads, 1)
            pool.wait_ge(s_pads, 2)
            for c in range(1, CHUNKS):
                pool.wait_ge(s_chunk_loaded[c], 16)
                pool.tensor_copy(chunk_hi[c][:, :], chunk_x[c][:, :]).then_inc(s_chunk_hi[c], 1)
                pool.wait_ge(s_chunk_hi[c], 1)
                pool.tensor_tensor(chunk_lo[c][:, :], chunk_x[c][:, :], chunk_hi[c][:, :].bitcast(fp32),
                                   ALU.subtract).then_inc(s_chunk_split[c], 1)

        @block.scalar
        def _(act):
            act.wait_ge(s_in_zero, 1)
            for q in range(4):
                r = q * QUAD
                act.dma_start(in_raw["f"][r:r + DELTA, :], w["fw_in"][0:DELTA, :]).then_inc(s_in_loaded, 16)
                act.dma_start(in_raw["p"][r + N_FLAT:r + FEATS, :], w["pw_in"]).then_inc(s_in_loaded, 16)
                act.dma_start(in_raw["f"][r + FEATS:r + FEATS + 1, :], w["fb_in"].rearrange("(a n) -> a n", a=1))\
                   .then_inc(s_in_loaded, 16)
                act.dma_start(in_raw["p"][r + FEATS:r + FEATS + 1, :], w["pb_in"].rearrange("(a n) -> a n", a=1))\
                   .then_inc(s_in_loaded, 16)
            for n in BIASES[:-1]:
                act.dma_start(bias[n][:, :], w[n].rearrange("(p a) -> p a", a=1)).then_inc(s_b_loaded, 16)
            act.dma_start(bias["cb2"][:, :], w["cb2"].rearrange("(p a) -> p a", a=1).to_broadcast([HID, 1]))\
               .then_inc(s_b_loaded, 16)
            act.dma_start(cw2_col[:, :], w["cw2"]).then_inc(s_b_loaded, 16)
            act.dma_start(delta_w[:, :], w["fw_in"][DELTA, :].rearrange("(p a) -> p a", a=1))\
               .then_inc(s_b_loaded, 16)
            act.preload_act_table(ACT.Sigmoid)
            act.wait_ge(s_b_loaded, N_B)

            def path_in(k):
                act.wait_ge(s_p_in_mm, k + 1)
                act.activation(p_t1[:, :], ps_path1[:, :], ACT.Identity).then_inc(s_p_in_t, 1)

            def path_1a(k):
                act.wait_ge(s_p1a_mm, k + 1)
                act.activation(p_t1[:, :], ps_path1[:, :], ACT.Identity,
                               bias=bias["pr1_b1"][:, :]).then_inc(s_p1a_t, 1)

            def path_2a(k):
                act.wait_ge(s_p2a_mm, k + 1)
                act.activation(p_t2[:, :], ps_path2[:, :], ACT.Identity,
                               bias=bias["pr2_b1"][:, :]).then_inc(s_p2a_t, 1)

            path_in(0)
            path_1a(0)
            path_in(1)
            path_2a(0)
            path_1a(1)

            def step(k, par, ahead1, ahead2):
                for g in range(GROUPS):
                    act.wait_ge(s_f1a_mm[g], k + 1)
                    act.activation(f_t[g][:, :], layer(ps_flat, g), ACT.Identity,
                                   bias=bias["fr1_b1"][:, :]).then_inc(s_f1a_t[g], 1)
                if ahead1:
                    path_in(k + 2)
                if ahead2:
                    path_2a(k + 1)
                for g in range(GROUPS):
                    act.wait_ge(s_f2a_mm[g], k + 1)
                    act.activation(f_t[g][:, :], layer(ps_flat, g), ACT.Identity,
                                   bias=bias["fr2_b1"][:, :]).then_inc(s_f2a_t[g], 1)
                if ahead1:
                    path_1a(k + 2)
                for g in range(GROUPS):
                    act.wait_ge(s_head_mm[g], k + 1)
                    act.activation(f_t[g][:, :], layer(ps_head, g), ACT.Identity,
                                   bias=bias["cb1"][:, :]).then_inc(s_head_t[g], 1)
                if not (isinstance(k, int) and k < 1):
                    act.wait_ge(s_stored, 16 * k)
                for g in range(GROUPS):
                    act.wait_ge(s_out_mm[g], k + 1)
                    act.activation(cols(delta[par], g), second(ps_head, g), ACT.Sigmoid,
                                   bias=bias["cb2"][:, :]).then_inc(s_delta[g], 1)

            over_steps(act, step)

        @block.vector
        def _(dve):
            dve.wait_ge(s_chunk_loaded[0], 16)
            dve.tensor_copy(chunk_hi[0][:, :], chunk_x[0][:, :]).then_inc(s_chunk_hi[0], 1)
            dve.wait_ge(s_chunk_hi[0], 1)
            dve.tensor_tensor(chunk_lo[0][:, :], chunk_x[0][:, :], chunk_hi[0][:, :].bitcast(fp32),
                              ALU.subtract).then_inc(s_chunk_split[0], 1)
            dve.wait_ge(s_in_loaded, N_IN)
            for t in "fp":
                dve.tensor_copy(in_split[t][:, :], in_raw[t][:, :]).then_inc(s_in_hi, 1)
            dve.wait_ge(s_in_hi, 2)
            for t in "fp":
                for q in (1, 3):
                    rows = slice(q * QUAD, (q + 1) * QUAD)
                    dve.tensor_tensor(in_split[t][rows, :], in_raw[t][rows, :],
                                      in_split[t][rows, :].bitcast(fp32), ALU.subtract).then_inc(s_in_split, 1)
            dve.wait_ge(s_b_loaded, N_B)
            dve.tensor_copy(cw2_rep[:, :], cw2_col[:, :].to_broadcast([HID, HID])).then_inc(s_cw2, 1)

            def leaky(dst, src):
                return dve.scalar_tensor_tensor(dst, src, NEG, src, ALU.mult, ALU.max)

            def path_in(k):
                dve.wait_ge(s_p_in_t, k + 1)
                leaky(p_in[:, :], p_t1[:, :]).then_inc(s_p_in_h, 1)

            def path_1a(k):
                dve.wait_ge(s_p1a_t, k + 1)
                leaky(p_mid1[:, :], p_t1[:, :]).then_inc(s_p1a_h, 1)

            def path_1b(k, par):
                dve.wait_ge(s_p1b_mm, k + 1)
                dve.scalar_tensor_tensor(p_sum1[:, :], ps_path1[:, :], bias["pr1_b2"][:, :], p_in[:, :],
                                         ALU.add, ALU.add).then_inc(s_p1b_t, 1)
                dve.wait_ge(s_p1b_t, k + 1)
                leaky(p_res1[par][:, :], p_sum1[:, :]).then_inc(s_p1b_h, 1)

            def path_2a(k):
                dve.wait_ge(s_p2a_t, k + 1)
                leaky(p_mid2[:, :], p_t2[:, :]).then_inc(s_p2a_h, 1)

            def path_2b(k, par):
                dve.wait_ge(s_p2b_mm, k + 1)
                dve.scalar_tensor_tensor(p_sum2[:, :], ps_path2[:, :], bias["pr2_b2"][:, :], p_res1[par][:, :],
                                         ALU.add, ALU.add).then_inc(s_p2b_t, 1)
                dve.wait_ge(s_p2b_t, k + 1)
                leaky(p_res2[par][:, :], p_sum2[:, :]).then_inc(s_p2b_h, 1)

            path_in(0)
            path_1a(0)
            path_1b(0, 0)
            path_in(1)
            path_2a(0)
            path_1a(1)
            path_2b(0, 0)
            path_1b(1, 1)
            dve.wait_ge(s_delta0, 16)

            def flat_in(k, par, g):
                dve.wait_ge(s_f_in_mm[g], k + 1)
                if not (isinstance(k, int) and k < 1):
                    dve.wait_ge(s_delta[g], k)
                dve.scalar_tensor_tensor(f_t[g][:, :], cols(delta[1 - par], g), delta_w[:, :],
                                         second(ps_flat, g), ALU.mult, ALU.add).then_inc(s_f_in_t[g], 1)
                dve.wait_ge(s_f_in_t[g], k + 1)
                leaky(f_in[g][:, :], f_t[g][:, :]).then_inc(s_f_in_h[g], 1)

            def flat_mid(k, g, t_done, dst, done):
                dve.wait_ge(t_done[g], k + 1)
                leaky(dst[g][:, :], f_t[g][:, :]).then_inc(done[g], 1)

            def flat_res(k, g, mm_done, b, old, t_done, dst, done):
                dve.wait_ge(mm_done[g], k + 1)
                dve.scalar_tensor_tensor(f_t[g][:, :], layer(ps_flat, g), bias[b][:, :], old[g][:, :],
                                         ALU.add, ALU.add).then_inc(t_done[g], 1)
                dve.wait_ge(t_done[g], k + 1)
                leaky(dst[g][:, :], f_t[g][:, :]).then_inc(done[g], 1)

            def step(k, par, ahead1, ahead2):
                for g in range(GROUPS):
                    flat_in(k, par, g)
                for g in range(GROUPS):
                    flat_mid(k, g, s_f1a_t, f_mid1, s_f1a_h)
                if ahead1:
                    path_in(k + 2)
                for g in range(GROUPS):
                    flat_res(k, g, s_f1b_mm, "fr1_b2", f_in, s_f1b_t, f_res1, s_f1b_h)
                if ahead2:
                    path_2a(k + 1)
                for g in range(GROUPS):
                    flat_mid(k, g, s_f2a_t, f_mid2, s_f2a_h)
                if ahead1:
                    path_1a(k + 2)
                for g in range(GROUPS):
                    flat_res(k, g, s_f2b_mm, "fr2_b2", f_res1, s_f2b_t, f_res2, s_f2b_h)
                if ahead2:
                    path_2b(k + 1, 1 - par)
                for g in range(GROUPS):
                    flat_mid(k, g, s_head_t, head, s_head_h)
                if ahead1:
                    path_1b(k + 2, par)

            over_steps(dve, step)

        @block.tensor
        def _(pe):
            def half(name, bank_, src, g):
                return pe.matmul(cols(bank_, g), hidden[name][:, :], cols(src, g), start=True, stop=True)

            def path_in(k, par):
                pe.wait_ge(s_x_loaded[par], 32 * k + (64 if par == 0 else 32))
                if not (isinstance(k, int) and k < 1):
                    pe.wait_ge(s_p1b_t, k)
                pe.matmul(ps_path1[:, :], in_split["p"][:, :], x_split[par][:, :],
                          start=True, stop=True).then_inc(s_p_in_mm, 1)

            def path_1a(k):
                pe.wait_ge(s_p_in_h, k + 1)
                half("pr1_w1", ps_path1, p_in, 0)
                half("pr1_w1", ps_path1, p_in, 1).then_inc(s_p1a_mm, 1)

            def path_1b(k):
                pe.wait_ge(s_p1a_h, k + 1)
                half("pr1_w2", ps_path1, p_mid1, 0)
                half("pr1_w2", ps_path1, p_mid1, 1).then_inc(s_p1b_mm, 1)

            def path_2a_first(k, par):
                pe.wait_ge(s_p1b_h, k + 1)
                if not (isinstance(k, int) and k < 1):
                    pe.wait_ge(s_p2b_t, k)
                half("pr2_w1", ps_path2, p_res1[par], 0)

            def path_2a_second(par):
                half("pr2_w1", ps_path2, p_res1[par], 1).then_inc(s_p2a_mm, 1)

            def path_2b(k):
                pe.wait_ge(s_p2a_h, k + 1)
                half("pr2_w2", ps_path2, p_mid2, 0)
                half("pr2_w2", ps_path2, p_mid2, 1).then_inc(s_p2b_mm, 1)

            def features(g, par):
                pe.matmul(second(ps_flat, g), in_split["f"][:, :], cols(x_split[par], g),
                          start=True, stop=True).then_inc(s_f_in_mm[g], 1)

            def combine_path(k, par, g):
                pe.wait_ge(s_p2b_h, k + 1)
                pe.matmul(layer(ps_head, g), comb_path[:, :], cols(p_res2[par], g), start=True, stop=False)

            def flat(k, g, ready, name, src, done):
                pe.wait_ge(ready[g], k + 1)
                pe.matmul(layer(ps_flat, g), hidden[name][:, :], src[g][:, :],
                          start=True, stop=True).then_inc(done[g], 1)

            pe.wait_ge(s_in_split, 4)
            path_in(0, 0)
            pe.wait_ge(s_w_loaded, N_W)
            path_1a(0)
            path_1b(0)
            path_in(1, 1)
            path_2a_first(0, 0)
            path_2a_second(0)
            path_1a(1)
            path_2b(0)
            for g in range(GROUPS):
                features(g, 0)
            path_1b(1)
            pe.wait_ge(s_cw2, 1)

            def step(k, par, ahead1, ahead2):
                for g in range(GROUPS):
                    flat(k, g, s_f_in_h, "fr1_w1", f_in, s_f1a_mm)
                if ahead1:
                    path_in(k + 2, par)
                if ahead2:
                    path_2a_first(k + 1, 1 - par)
                for g in range(GROUPS):
                    flat(k, g, s_f1a_h, "fr1_w2", f_mid1, s_f1b_mm)
                if ahead2:
                    path_2a_second(1 - par)
                combine_path(k, par, 0)
                for g in range(GROUPS):
                    flat(k, g, s_f1b_h, "fr2_w1", f_res1, s_f2a_mm)
                combine_path(k, par, 1)
                if ahead1:
                    path_1a(k + 2)
                for g in range(GROUPS):
                    flat(k, g, s_f2a_h, "fr2_w2", f_mid2, s_f2b_mm)
                if ahead2:
                    path_2b(k + 1)
                for g in range(GROUPS):
                    pe.wait_ge(s_f2b_h[g], k + 1)
                    pe.matmul(layer(ps_head, g), comb_flat[:, :], f_res2[g][:, :],
                              start=False, stop=True).then_inc(s_head_mm[g], 1)
                if ahead2:
                    for g in range(GROUPS):
                        features(g, 1 - par)
                for g in range(GROUPS):
                    pe.wait_ge(s_head_h[g], k + 1)
                    pe.matmul(second(ps_head, g), cw2_rep[:, :], head[g][:, :],
                              start=True, stop=True).then_inc(s_out_mm[g], 1)
                if ahead1:
                    path_1b(k + 2)

            over_steps(pe, step)


def kernel(**inputs):
    import concourse.bacc as bacc
    from concourse.bass_utils import run_bass_kernel_spmd

    nc = bacc.Bacc("TRN2", target_bir_lowering=False, num_devices=1)
    x_host = np.ascontiguousarray(np.transpose(inputs["r_feats"], (1, 2, 0)))
    arrays = {"x": x_host}
    x = nc.dram_tensor("x", x_host.shape, mybir.dt.float32, kind="ExternalInput").ap()
    w = {}
    for name in inputs:
        if name != "r_feats":
            short = name.replace("L0_rec_", "")
            arrays["in_" + short] = np.ascontiguousarray(inputs[name])
            w[short] = nc.dram_tensor("in_" + short, arrays["in_" + short].shape, mybir.dt.float32,
                                      kind="ExternalInput").ap()
    out = nc.dram_tensor("out", (STEPS, BATCH), mybir.dt.float32, kind="ExternalOutput").ap()
    x_hi = nc.dram_tensor("x_hi", x_host.shape, mybir.dt.float32, kind="Internal").ap()
    x_lo = nc.dram_tensor("x_lo", x_host.shape, mybir.dt.float32, kind="Internal").ap()
    build(nc, x, x_hi, x_lo, w, out)
    result = run_bass_kernel_spmd(nc, [arrays], core_ids=[0])
    return np.ascontiguousarray(np.transpose(result.results[0]["out"], (1, 0)))
```

```python
import numpy as np

import concourse.bass as bass
from concourse import mybir
from contextlib import ExitStack

STEPS, BATCH, FEATS, HID = 128, 512, 12, 128
N_FLAT, DELTA = 4, 3
NEG = 0.2
GROUPS = 2
G = BATCH // GROUPS
QUAD = 32
CHUNK_STEPS = [8, 24, 48, 48]
CHUNKS = len(CHUNK_STEPS)
CHUNK_FIRST = [sum(CHUNK_STEPS[:c]) for c in range(CHUNKS)]
CHUNK_COLS = [n * FEATS * BATCH // 128 for n in CHUNK_STEPS]

HIDDEN = ["fr1_w1", "fr1_w2", "fr2_w1", "fr2_w2", "pr1_w1", "pr1_w2", "pr2_w1", "pr2_w2", "cw1_flat", "cw1_path",
          "fr1_w1_T"]
COLUMNS = ["fr1_b1", "fr1_b2", "fr2_b1", "fr2_b2", "pr1_b1", "pr1_b2", "pr2_b1", "pr2_b2", "cb1", "cw2", "delta_w"]
LEAD = 3


def build(nc, x, x_hi, x_lo, w, out):
    fp32, fp32r = mybir.dt.float32, mybir.dt.float32r
    ALU, ACT = mybir.AluOpType, mybir.ActivationFunctionType

    ctx = ExitStack()
    with ctx:
        def sb(name, shape, dt=fp32):
            return ctx.enter_context(nc.sbuf_tensor(name, shape, dt))

        def bank(name):
            return ctx.enter_context(nc.psum_tensor(name, [128, 512], fp32))

        def sem(name):
            return ctx.enter_context(nc.semaphore(name))

        def per_group(name):
            return [sem(f"{name}_{g}") for g in range(GROUPS)]

        hidden_w = sb("hidden_w", [HID, len(HIDDEN) * HID])
        weight = {n: hidden_w[:, i * HID:(i + 1) * HID] for i, n in enumerate(HIDDEN)}
        columns_sb = sb("columns_sb", [HID, len(COLUMNS)])
        column = {n: columns_sb[:, i:i + 1] for i, n in enumerate(COLUMNS)}
        cb2_col, cw2_rep = sb("cb2_col", [HID, 1]), sb("cw2_rep", [HID, HID])
        identity_w, skip_w = sb("identity_w", [HID, HID]), sb("skip_w", [HID, HID])
        skip_b, relu_b = sb("skip_b", [HID, 1]), sb("relu_b", [HID, 1])
        in_raw, in_split = sb("in_raw", [128, 2 * HID]), sb("in_split", [128, 2 * HID], fp32r)
        flat_in_w, path_in_w = in_split[:, 0:HID], in_split[:, HID:2 * HID]
        chunk_x = [sb(f"chunk_x{c}", [128, CHUNK_COLS[c]]) for c in range(CHUNKS)]
        chunk_hi = [sb(f"chunk_hi{c}", [128, CHUNK_COLS[c]], fp32r) for c in range(CHUNKS)]
        chunk_lo = [sb(f"chunk_lo{c}", [128, CHUNK_COLS[c]], fp32r) for c in range(CHUNKS)]
        x_flat = [sb(f"x_flat{p}", [128, BATCH], fp32r) for p in range(2)]
        x_path = [sb(f"x_path{p}", [128, BATCH], fp32r) for p in range(2)]
        p_in, p_mid1, p_mid2 = sb("p_in", [HID, BATCH]), sb("p_mid1", [HID, BATCH]), sb("p_mid2", [HID, BATCH])
        p_t1, p_t2 = sb("p_t1", [HID, BATCH]), sb("p_t2", [HID, BATCH])
        p_sum1, p_sum2 = sb("p_sum1", [HID, BATCH]), sb("p_sum2", [HID, BATCH])
        p_res1 = [sb(f"p_res1_{p}", [HID, BATCH]) for p in range(2)]
        p_res2 = [sb(f"p_res2_{p}", [HID, BATCH]) for p in range(2)]
        f_t, f_in, f_mid1, f_mid2, f_res1, f_res2, head = (
            [sb(f"{n}_{g}", [HID, G]) for g in range(GROUPS)]
            for n in ("f_t", "f_in", "f_mid1", "f_mid2", "f_res1", "f_res2", "head"))
        delta = [sb(f"delta{p}", [HID, BATCH]) for p in range(2)]

        ps_flat = [bank(f"ps_flat{g}") for g in range(GROUPS)]
        ps_block = [bank(f"ps_block{g}") for g in range(GROUPS)]
        ps_head = [bank(f"ps_head{g}") for g in range(GROUPS)]
        ps_path1, ps_path2 = bank("ps_path1"), bank("ps_path2")

        def layer(b, g):
            return b[g][:, 0:G]

        def second(b, g):
            return b[g][:, G:2 * G]

        def cols(t, g):
            return t[:, g * G:(g + 1) * G]

        s_in_zero, s_pads, s_in_loaded, s_in_hi, s_in_split = (
            sem(n) for n in ("s_in_zero", "s_pads", "s_in_loaded", "s_in_hi", "s_in_split"))
        s_w_loaded, s_columns, s_cw2, s_delta0 = (sem(n) for n in ("s_w_loaded", "s_columns", "s_cw2", "s_delta0"))
        s_identity, s_skip_mm, s_skip = sem("s_identity"), sem("s_skip_mm"), sem("s_skip")
        s_chunk_loaded, s_chunk_hi, s_chunk_split, s_chunk_stored = (
            [sem(f"{n}{c}") for c in range(CHUNKS)]
            for n in ("s_chunk_loaded", "s_chunk_hi", "s_chunk_split", "s_chunk_stored"))
        s_x_flat = [sem(f"s_x_flat{p}") for p in range(2)]
        s_x_path = [sem(f"s_x_path{p}") for p in range(2)]
        s_stored = sem("s_stored")
        s_p_in_mm, s_p_in_t, s_p_in_h, s_p1a_mm, s_p1a_t, s_p1a_h, s_p1b_mm, s_p1b_t, s_p1b_h = (sem(n) for n in (
            "s_p_in_mm", "s_p_in_t", "s_p_in_h", "s_p1a_mm", "s_p1a_t", "s_p1a_h", "s_p1b_mm", "s_p1b_t", "s_p1b_h"))
        s_p2a_mm, s_p2a_t, s_p2a_h, s_p2b_mm, s_p2b_t, s_p2b_h = (sem(n) for n in (
            "s_p2a_mm", "s_p2a_t", "s_p2a_h", "s_p2b_mm", "s_p2b_t", "s_p2b_h"))
        s_f_in_mm, s_f_in_t, s_f_in_h, s_f1a_mm, s_f1a_h, s_f1b_mm, s_f1b_t, s_f1b_h = (
            per_group(n) for n in ("s_f_in_mm", "s_f_in_t", "s_f_in_h", "s_f1a_mm", "s_f1a_h",
                                   "s_f1b_mm", "s_f1b_t", "s_f1b_h"))
        s_f2a_mm, s_f2a_t, s_f2a_h, s_f2b_mm, s_f2b_t, s_f2b_h = (
            per_group(n) for n in ("s_f2a_mm", "s_f2a_t", "s_f2a_h", "s_f2b_mm", "s_f2b_t", "s_f2b_h"))
        s_head_mm, s_head_t, s_head_h, s_out_mm, s_delta = (
            per_group(n) for n in ("s_head_mm", "s_head_t", "s_head_h", "s_out_mm", "s_delta"))

        def chunk_rows(features, c):
            return features[CHUNK_FIRST[c]:CHUNK_FIRST[c] + CHUNK_STEPS[c], :, :]\
                .rearrange("s f b -> (s f b)").rearrange("(r n) -> r n", n=CHUNK_COLS[c])

        block = ctx.enter_context(nc.Block())

        def exists(k):
            return not isinstance(k, int) or 0 <= k < STEPS

        def bodies(eng, body):
            for k in range(-LEAD, 2):
                body(k, k % 2)
            with eng.Fori(2, STEPS - 5, 2) as k:
                body(k, 0)
                body(k + 1, 1)
            for k in range(STEPS - 4, STEPS):
                body(k, k % 2)

        @block.sync
        def _(sp):
            def load_x(tile, loaded, rows, k, par):
                for q, part in enumerate((x_hi, x_hi, x_lo, x_lo)):
                    sp.dma_start(tile[par][q * QUAD + rows.start:q * QUAD + rows.stop, :].bitcast(fp32),
                                 part[bass.ds(k, 1), rows, :].rearrange("a f b -> (a f) b")).then_inc(loaded[par], 16)

            def load_path(k, par):
                if not exists(k):
                    return
                if exists(k - 2):
                    sp.wait_ge(s_p_in_mm, k - 1)
                load_x(x_path, s_x_path, slice(N_FLAT, FEATS), k, par)

            def load_flat(k, par):
                if not exists(k):
                    return
                if exists(k - 2):
                    for g in range(GROUPS):
                        sp.wait_ge(s_f_in_mm[g], k - 1)
                load_x(x_flat, s_x_flat, slice(0, DELTA), k, par)

            def store_delta(k, par):
                if not exists(k):
                    return
                for g in range(GROUPS):
                    sp.wait_ge(s_delta[g], k + 1)
                sp.dma_start(out[bass.ds(k, 1), :], delta[par][0:1, :]).then_inc(s_stored, 16)

            def load_chunk(c):
                sp.dma_start(chunk_x[c][:, :], chunk_rows(x, c)).then_inc(s_chunk_loaded[c], 16)

            def store_chunk(c):
                sp.wait_ge(s_chunk_split[c], 1)
                sp.dma_start(chunk_rows(x_hi, c),
                             chunk_hi[c][:, :].bitcast(fp32)).then_inc(s_chunk_stored[c], 16)
                sp.dma_start(chunk_rows(x_lo, c),
                             chunk_lo[c][:, :].bitcast(fp32)).then_inc(s_chunk_stored[c], 16)

            def body(k, par):
                load_path(k, par)
                load_flat(k - 2, par)
                store_delta(k - 5, 1 - par)

            load_chunk(0)
            sp.wait_ge(s_in_zero, 1)
            for q in range(4):
                sp.dma_start(in_raw[q * QUAD:q * QUAD + FEATS + 1, :], w["inputs"]).then_inc(s_in_loaded, 16)
            sp.dma_start(hidden_w[:, :], w["hidden"]).then_inc(s_w_loaded, 16)
            sp.dma_start(delta[1][:, :], x[0, DELTA:DELTA + 1, :].to_broadcast([HID, BATCH])).then_inc(s_delta0, 16)
            store_chunk(0)
            sp.wait_ge(s_pads, 2)
            sp.wait_ge(s_chunk_stored[0], 32)
            body(0, 0)
            body(1, 1)
            for c in range(1, CHUNKS):
                load_chunk(c)
            for k in range(2, 6):
                body(k, k % 2)
            for c in range(1, CHUNKS):
                store_chunk(c)
            for c in range(CHUNKS):
                sp.wait_ge(s_chunk_stored[c], 32)
                with sp.Fori(max(6, CHUNK_FIRST[c]), CHUNK_FIRST[c] + CHUNK_STEPS[c] - 1, 2) as k:
                    body(k, 0)
                    body(k + 1, 1)
            for k in range(STEPS, STEPS + 5):
                body(k, k % 2)
            sp.wait_ge(s_stored, 16 * STEPS)

        @block.gpsimd
        def _(pool):
            pool.memset(in_raw[:, :], 0.0).then_inc(s_in_zero, 1)
            for tile in x_flat + x_path:
                last = pool.memset(tile[:, :].bitcast(fp32), 0.0)
            last.then_inc(s_pads, 1)
            pool.memset(identity_w[:, :], 0.0).then_inc(s_identity, 1)
            pool.wait_ge(s_identity, 1)
            pool.affine_select(out=identity_w[:, :], in_=identity_w[:, :], compare_op=ALU.not_equal, fill=1.0,
                               base=0, pattern=[[-1, HID]], channel_multiplier=1).then_inc(s_identity, 1)
            pool.wait_ge(s_pads, 1)
            for tile in x_flat + x_path:
                last = pool.memset(tile[0:2 * QUAD, :].bitcast(fp32), 1.0)
            last.then_inc(s_pads, 1)
            pool.wait_ge(s_pads, 2)
            for c in range(1, CHUNKS):
                pool.wait_ge(s_chunk_loaded[c], 16)
                pool.tensor_copy(chunk_hi[c][:, :], chunk_x[c][:, :]).then_inc(s_chunk_hi[c], 1)
                pool.wait_ge(s_chunk_hi[c], 1)
                pool.tensor_tensor(chunk_lo[c][:, :], chunk_x[c][:, :], chunk_hi[c][:, :].bitcast(fp32),
                                   ALU.subtract).then_inc(s_chunk_split[c], 1)

        @block.scalar
        def _(act):
            act.dma_start(columns_sb[:, :], w["columns"]).then_inc(s_columns, 16)
            act.dma_start(cb2_col[:, :], w["cb2"].rearrange("(p a) -> p a", a=1).to_broadcast([HID, 1]))\
               .then_inc(s_columns, 16)
            act.preload_act_table(ACT.Sigmoid)
            act.wait_ge(s_columns, 32)

            def identity(dst, src, bias):
                return act.activation(dst, src, ACT.Identity, bias=bias)

            def path_in(k):
                if exists(k):
                    act.wait_ge(s_p_in_mm, k + 1)
                    act.activation(p_t1[:, :], ps_path1[:, :], ACT.Identity).then_inc(s_p_in_t, 1)

            def path_1a(k):
                if exists(k):
                    act.wait_ge(s_p1a_mm, k + 1)
                    identity(p_t1[:, :], ps_path1[:, :], column["pr1_b1"]).then_inc(s_p1a_t, 1)

            def path_2a(k):
                if exists(k):
                    act.wait_ge(s_p2a_mm, k + 1)
                    identity(p_t2[:, :], ps_path2[:, :], column["pr2_b1"]).then_inc(s_p2a_t, 1)

            def flat_1a(k, g):
                if exists(k):
                    act.wait_ge(s_f1a_mm[g], k + 1)
                    act.activation(f_mid1[g][:, :], layer(ps_flat, g), ACT.Relu, bias=relu_b[:, :],
                                   scale=1.0 - NEG).then_inc(s_f1a_h[g], 1)

            def flat_1b(k, g):
                if exists(k):
                    act.wait_ge(s_f1b_mm[g], k + 1)
                    identity(f_t[g][:, :], layer(ps_block, g), skip_b[:, :]).then_inc(s_f1b_t[g], 1)

            def flat_2a(k, g):
                if exists(k):
                    act.wait_ge(s_f2a_mm[g], k + 1)
                    identity(f_t[g][:, :], layer(ps_flat, g), column["fr2_b1"]).then_inc(s_f2a_t[g], 1)

            def combine(k, g):
                if exists(k):
                    act.wait_ge(s_head_mm[g], k + 1)
                    identity(f_t[g][:, :], layer(ps_head, g), column["cb1"]).then_inc(s_head_t[g], 1)

            def output(k, par, g):
                if exists(k):
                    act.wait_ge(s_out_mm[g], k + 1)
                    if exists(k - 1):
                        act.wait_ge(s_stored, 16 * k)
                    act.activation(cols(delta[par], g), second(ps_head, g), ACT.Sigmoid,
                                   bias=cb2_col[:, :]).then_inc(s_delta[g], 1)

            def body(k, par):
                flat_1a(k, 0)
                path_2a(k + 1)
                flat_1a(k, 1)
                flat_1b(k, 0)
                flat_1b(k, 1)
                flat_2a(k, 0)
                path_1a(k + 2)
                flat_2a(k, 1)
                combine(k, 0)
                combine(k, 1)
                output(k, par, 0)
                path_in(k + 3)
                output(k, par, 1)

            act.wait_ge(s_skip, 3)
            bodies(act, body)

        @block.vector
        def _(dve):
            dve.wait_ge(s_chunk_loaded[0], 16)
            dve.tensor_copy(chunk_hi[0][:, :], chunk_x[0][:, :]).then_inc(s_chunk_hi[0], 1)
            dve.wait_ge(s_chunk_hi[0], 1)
            dve.tensor_tensor(chunk_lo[0][:, :], chunk_x[0][:, :], chunk_hi[0][:, :].bitcast(fp32),
                              ALU.subtract).then_inc(s_chunk_split[0], 1)
            dve.wait_ge(s_in_loaded, 64)
            dve.tensor_copy(in_split[:, :], in_raw[:, :]).then_inc(s_in_hi, 1)
            dve.wait_ge(s_in_hi, 1)
            for q in (1, 3):
                rows = slice(q * QUAD, (q + 1) * QUAD)
                dve.tensor_tensor(in_split[rows, :], in_raw[rows, :], in_split[rows, :].bitcast(fp32),
                                  ALU.subtract).then_inc(s_in_split, 1)
            dve.wait_ge(s_columns, 32)
            dve.tensor_copy(cw2_rep[:, :], column["cw2"].to_broadcast([HID, HID])).then_inc(s_cw2, 1)

            dve.tensor_scalar(relu_b[:, :], column["fr1_b1"], 1.0 - NEG, None, ALU.mult).then_inc(s_skip, 1)
            dve.wait_ge(s_identity, 2)
            dve.wait_ge(s_skip_mm, 1)
            dve.scalar_tensor_tensor(skip_w[:, :], ps_block[0][:, 0:HID], NEG, identity_w[:, :],
                                     ALU.mult, ALU.add).then_inc(s_skip, 1)
            dve.scalar_tensor_tensor(skip_b[:, :], ps_block[0][:, HID:HID + 1], NEG, column["fr1_b2"],
                                     ALU.mult, ALU.add).then_inc(s_skip, 1)

            def leaky(dst, src):
                return dve.scalar_tensor_tensor(dst, src, NEG, src, ALU.mult, ALU.max)

            def add(dst, products, bias, old):
                return dve.scalar_tensor_tensor(dst, products, bias, old, ALU.add, ALU.add)

            def path_in(k):
                if exists(k):
                    dve.wait_ge(s_p_in_t, k + 1)
                    leaky(p_in[:, :], p_t1[:, :]).then_inc(s_p_in_h, 1)

            def path_1a(k):
                if exists(k):
                    dve.wait_ge(s_p1a_t, k + 1)
                    leaky(p_mid1[:, :], p_t1[:, :]).then_inc(s_p1a_h, 1)

            def path_1b_sum(k):
                if exists(k):
                    dve.wait_ge(s_p1b_mm, k + 1)
                    add(p_sum1[:, :], ps_path1[:, :], column["pr1_b2"], p_in[:, :]).then_inc(s_p1b_t, 1)

            def path_1b(k, par):
                if exists(k):
                    dve.wait_ge(s_p1b_t, k + 1)
                    leaky(p_res1[par][:, :], p_sum1[:, :]).then_inc(s_p1b_h, 1)

            def path_2a(k):
                if exists(k):
                    dve.wait_ge(s_p2a_t, k + 1)
                    leaky(p_mid2[:, :], p_t2[:, :]).then_inc(s_p2a_h, 1)

            def path_2b_sum(k, par):
                if exists(k):
                    dve.wait_ge(s_p2b_mm, k + 1)
                    add(p_sum2[:, :], ps_path2[:, :], column["pr2_b2"], p_res1[par][:, :]).then_inc(s_p2b_t, 1)

            def path_2b(k, par):
                if exists(k):
                    dve.wait_ge(s_p2b_t, k + 1)
                    leaky(p_res2[par][:, :], p_sum2[:, :]).then_inc(s_p2b_h, 1)

            def flat_in(k, par, g):
                if exists(k):
                    if exists(k - 1):
                        dve.wait_ge(s_delta[g], k)
                    else:
                        dve.wait_ge(s_delta0, 16)
                    dve.wait_ge(s_f_in_mm[g], k + 1)
                    dve.scalar_tensor_tensor(f_t[g][:, :], cols(delta[1 - par], g), column["delta_w"],
                                             second(ps_flat, g), ALU.mult, ALU.add).then_inc(s_f_in_t[g], 1)
                    dve.wait_ge(s_f_in_t[g], k + 1)
                    leaky(f_in[g][:, :], f_t[g][:, :]).then_inc(s_f_in_h[g], 1)

            def flat_1b(k, g):
                if exists(k):
                    dve.wait_ge(s_f1b_t[g], k + 1)
                    leaky(f_res1[g][:, :], f_t[g][:, :]).then_inc(s_f1b_h[g], 1)

            def flat_2a(k, g):
                if exists(k):
                    dve.wait_ge(s_f2a_t[g], k + 1)
                    leaky(f_mid2[g][:, :], f_t[g][:, :]).then_inc(s_f2a_h[g], 1)

            def flat_2b(k, g):
                if exists(k):
                    dve.wait_ge(s_f2b_mm[g], k + 1)
                    add(f_t[g][:, :], layer(ps_flat, g), column["fr2_b2"], f_res1[g][:, :]).then_inc(s_f2b_t[g], 1)
                    dve.wait_ge(s_f2b_t[g], k + 1)
                    leaky(f_res2[g][:, :], f_t[g][:, :]).then_inc(s_f2b_h[g], 1)

            def combine(k, g):
                if exists(k):
                    dve.wait_ge(s_head_t[g], k + 1)
                    leaky(head[g][:, :], f_t[g][:, :]).then_inc(s_head_h[g], 1)

            def body(k, par):
                flat_in(k, par, 0)
                flat_in(k, par, 1)
                path_in(k + 2)
                path_2b(k, par)
                path_2a(k + 1)
                flat_1b(k, 0)
                flat_1b(k, 1)
                flat_2a(k, 0)
                path_1a(k + 2)
                flat_2a(k, 1)
                flat_2b(k, 0)
                flat_2b(k, 1)
                path_1b_sum(k + 2)
                combine(k, 0)
                path_1b(k + 2, par)
                combine(k, 1)
                path_2b_sum(k + 1, 1 - par)

            bodies(dve, body)

        @block.tensor
        def _(pe):
            def product(dst, w_name, src):
                return pe.matmul(dst, weight[w_name], src, start=True, stop=True)

            def filled(k, par):
                return 32 * k + (64 if par == 0 else 32)

            def path_in(k, par):
                if exists(k):
                    pe.wait_ge(s_x_path[par], filled(k, par))
                    if exists(k - 1):
                        pe.wait_ge(s_p1b_t, k)
                    pe.matmul(ps_path1[:, :], path_in_w, x_path[par][:, :], start=True, stop=True)\
                      .then_inc(s_p_in_mm, 1)

            def path_1a(k, g):
                if exists(k):
                    if g == 0:
                        pe.wait_ge(s_p_in_h, k + 1)
                        product(cols(ps_path1, g), "pr1_w1", cols(p_in, g))
                    else:
                        product(cols(ps_path1, g), "pr1_w1", cols(p_in, g)).then_inc(s_p1a_mm, 1)

            def path_1b(k, g):
                if exists(k):
                    if g == 0:
                        pe.wait_ge(s_p1a_h, k + 1)
                        product(cols(ps_path1, g), "pr1_w2", cols(p_mid1, g))
                    else:
                        product(cols(ps_path1, g), "pr1_w2", cols(p_mid1, g)).then_inc(s_p1b_mm, 1)

            def path_2a(k, par, g):
                if exists(k):
                    if g == 0:
                        pe.wait_ge(s_p1b_h, k + 1)
                        if exists(k - 1):
                            pe.wait_ge(s_p2b_t, k)
                        product(cols(ps_path2, g), "pr2_w1", cols(p_res1[par], g))
                    else:
                        product(cols(ps_path2, g), "pr2_w1", cols(p_res1[par], g)).then_inc(s_p2a_mm, 1)

            def path_2b(k, g):
                if exists(k):
                    if g == 0:
                        pe.wait_ge(s_p2a_h, k + 1)
                        product(cols(ps_path2, g), "pr2_w2", cols(p_mid2, g))
                    else:
                        product(cols(ps_path2, g), "pr2_w2", cols(p_mid2, g)).then_inc(s_p2b_mm, 1)

            def flat_in(k, par, g):
                if exists(k):
                    pe.wait_ge(s_x_flat[par], filled(k, par))
                    pe.matmul(second(ps_flat, g), flat_in_w, cols(x_flat[par], g), start=True, stop=True)\
                      .then_inc(s_f_in_mm[g], 1)

            def flat_1a(k, g):
                if exists(k):
                    pe.wait_ge(s_f_in_h[g], k + 1)
                    product(layer(ps_flat, g), "fr1_w1", f_in[g][:, :]).then_inc(s_f1a_mm[g], 1)

            def flat_1_skip(k, g):
                if exists(k):
                    pe.matmul(layer(ps_block, g), skip_w[:, :], f_in[g][:, :], start=True, stop=False)

            def flat_1b(k, g):
                if exists(k):
                    pe.wait_ge(s_f1a_h[g], k + 1)
                    pe.matmul(layer(ps_block, g), weight["fr1_w2"], f_mid1[g][:, :], start=False, stop=True)\
                      .then_inc(s_f1b_mm[g], 1)

            def flat_2a(k, g):
                if exists(k):
                    pe.wait_ge(s_f1b_h[g], k + 1)
                    product(layer(ps_flat, g), "fr2_w1", f_res1[g][:, :]).then_inc(s_f2a_mm[g], 1)

            def flat_2b(k, g):
                if exists(k):
                    pe.wait_ge(s_f2a_h[g], k + 1)
                    product(layer(ps_flat, g), "fr2_w2", f_mid2[g][:, :]).then_inc(s_f2b_mm[g], 1)

            def combine_path(k, par, g):
                if exists(k):
                    pe.wait_ge(s_p2b_h, k + 1)
                    pe.matmul(layer(ps_head, g), weight["cw1_path"], cols(p_res2[par], g), start=True, stop=False)

            def combine_flat(k, g):
                if exists(k):
                    pe.wait_ge(s_f2b_h[g], k + 1)
                    pe.matmul(layer(ps_head, g), weight["cw1_flat"], f_res2[g][:, :], start=False, stop=True)\
                      .then_inc(s_head_mm[g], 1)

            def output(k, g):
                if exists(k):
                    pe.wait_ge(s_head_h[g], k + 1)
                    pe.matmul(second(ps_head, g), cw2_rep[:, :], head[g][:, :], start=True, stop=True)\
                      .then_inc(s_out_mm[g], 1)

            def body(k, par):
                flat_1a(k, 0)
                flat_1_skip(k, 0)
                flat_1a(k, 1)
                flat_1b(k, 0)
                path_1a(k + 2, 0)
                flat_1_skip(k, 1)
                flat_1b(k, 1)
                flat_2a(k, 0)
                path_1a(k + 2, 1)
                combine_path(k, par, 0)
                flat_2a(k, 1)
                combine_path(k, par, 1)
                flat_2b(k, 0)
                path_1b(k + 2, 0)
                flat_2b(k, 1)
                path_1b(k + 2, 1)
                combine_flat(k, 0)
                path_2b(k + 1, 0)
                combine_flat(k, 1)
                path_2b(k + 1, 1)
                flat_in(k + 1, 1 - par, 0)
                output(k, 0)
                flat_in(k + 1, 1 - par, 1)
                path_in(k + 3, 1 - par)
                output(k, 1)
                path_2a(k + 2, par, 0)
                path_2a(k + 2, par, 1)

            pe.wait_ge(s_w_loaded, 16)
            pe.wait_ge(s_columns, 32)
            pe.matmul(ps_block[0][:, 0:HID], weight["fr1_w1_T"], weight["fr1_w2"], start=True, stop=True)
            pe.matmul(ps_block[0][:, HID:HID + 1], weight["fr1_w2"], column["fr1_b1"], start=True, stop=True)\
              .then_inc(s_skip_mm, 1)
            pe.wait_ge(s_skip, 3)
            pe.wait_ge(s_in_split, 2)
            pe.wait_ge(s_cw2, 1)
            bodies(pe, body)


def kernel(**inputs):
    import concourse.bacc as bacc
    from concourse.bass_utils import run_bass_kernel_spmd

    nc = bacc.Bacc("TRN2", target_bir_lowering=False, num_devices=1)
    x_host = np.ascontiguousarray(np.transpose(inputs["r_feats"], (1, 2, 0)))
    given = {name.replace("L0_rec_", ""): a for name, a in inputs.items()}
    given["cw1_flat"], given["cw1_path"] = given["cw1"][0:HID], given["cw1"][HID:2 * HID]
    given["fr1_w1_T"] = np.transpose(given["fr1_w1"])
    given["delta_w"] = given["fw_in"][DELTA]
    hidden = np.concatenate([given[n] for n in HIDDEN], axis=1)
    columns = np.stack([np.reshape(given[n], (HID,)) for n in COLUMNS], axis=1)
    in_w = np.zeros((FEATS + 1, 2 * HID), np.float32)
    in_w[0:DELTA, 0:HID] = given["fw_in"][0:DELTA]
    in_w[N_FLAT:FEATS, HID:2 * HID] = given["pw_in"]
    in_w[FEATS, 0:HID], in_w[FEATS, HID:2 * HID] = given["fb_in"], given["pb_in"]
    arrays = {"x": x_host, "hidden": hidden, "columns": columns, "inputs": in_w, "cb2": np.asarray(given["cb2"])}
    dram = {n: nc.dram_tensor(n, a.shape, mybir.dt.float32, kind="ExternalInput").ap() for n, a in arrays.items()}
    x = dram.pop("x")
    x_hi = nc.dram_tensor("x_hi", x_host.shape, mybir.dt.float32, kind="Internal").ap()
    x_lo = nc.dram_tensor("x_lo", x_host.shape, mybir.dt.float32, kind="Internal").ap()
    out = nc.dram_tensor("out", (STEPS, BATCH), mybir.dt.float32, kind="ExternalOutput").ap()
    build(nc, x, x_hi, x_lo, dram, out)
    result = run_bass_kernel_spmd(nc, [arrays], core_ids=[0])
    return np.ascontiguousarray(np.transpose(result.results[0]["out"], (1, 0)))
```
